# Optimizing a Trainium2 kernel written in Bass

```python
import numpy as np
import jax
import jax.numpy as jnp

def _softmax(x, axis=-1):
    return jax.nn.softmax(x, axis=axis)

def _gelu(x):
    return jax.nn.gelu(x, approximate=True)

def _silu(x):
    return jax.nn.silu(x)

def _sigmoid(x):
    return jax.nn.sigmoid(x)

def _layernorm(x, axis=-1, eps=1e-05):
    m = jnp.mean(x, axis=axis, keepdims=True)
    v = jnp.var(x, axis=axis, keepdims=True)
    return (x - m) / jnp.sqrt(v + eps)

def _scatter_add(tgt, idx, src, axis=0):
    return tgt.at[idx].add(src)

def _segment_sum(src, seg, n):
    return jax.ops.segment_sum(src, seg, n)
kernel_name = 'mk_gnn_resnorm_d1_gnn_r32_bbb970'

def setup_inputs(seed: int=0):
    np.random.seed(seed)
    _w = jnp.asarray

    def _rec_inputs():
        import jax
        import jax.numpy as jnp
        _gk = jax.random.key(seed)
        x = -0.000202 + 1 * jax.random.normal(jax.random.fold_in(_gk, 1), (3125, 64), jnp.float32)
        _s = jax.random.randint(jax.random.fold_in(_gk, 2), (50000,), 0, 3125, jnp.int32)
        _d = jax.random.randint(jax.random.fold_in(_gk, 3), (50000,), 0, 3125, jnp.int32)
        _loop = jnp.arange(3125, dtype=jnp.int32)
        src = jnp.concatenate([_s, _d, _loop])
        dst = jnp.concatenate([_d, _s, _loop])
        _o = jnp.argsort(dst, stable=True)
        src = src[_o]
        dst = dst[_o]
        edge_attr_64 = -5.16925e-05 + 1.00005 * jax.random.normal(jax.random.fold_in(_gk, 11), (103125, 64), jnp.float32)
        return (x, src, dst, edge_attr_64)
    x, src, dst, edge_attr_64 = _rec_inputs()

    def _L0_gnn_setup():
        import jax, jax.numpy as jnp
        import numpy as np
        N = 3125
        E = 50000
        C = 64
        H = 64
        L = 4
        EPS_MSG = 1e-07
        LN_EPS = 1e-05

        def _layernorm(x, g, b):
            mu = jnp.mean(x, axis=-1, keepdims=True)
            var = jnp.mean(jnp.square(x - mu), axis=-1, keepdims=True)
            return (x - mu) * jax.lax.rsqrt(var + LN_EPS) * g + b

        def _genconv(h, edge_attr, src, dst, w1, b1, g1, bb1, w2, b2, t):
            msg = jax.nn.relu(h[src] + edge_attr) + EPS_MSG
            m = msg * t
            seg_max = jax.lax.stop_gradient(jax.ops.segment_max(m, dst, num_segments=N))
            ex = jnp.exp(m - seg_max[dst])
            denom = jax.ops.segment_sum(ex, dst, num_segments=N)
            alpha = ex / (denom[dst] + 1e-16)
            agg = jax.ops.segment_sum(msg * alpha, dst, num_segments=N)
            out = h + agg
            z = jax.nn.relu(_layernorm(out @ w1 + b1, g1, bb1))
            return z @ w2 + b2
        key = jax.random.key(seed)
        ks = jax.random.split(key, 16)
        s = 0.05
        return {'x': jax.random.normal(ks[0], (N, C), jnp.float32), 'edge_index': jax.random.randint(ks[1], (2, E), 0, N, jnp.int32), 'edge_attr': jax.random.normal(ks[2], (E, C), jnp.float32), 'enc_node_w': jax.random.normal(ks[3], (C, H), jnp.float32) * s, 'enc_node_b': jnp.zeros((H,), jnp.float32), 'enc_edge_w': jax.random.normal(ks[4], (C, H), jnp.float32) * s, 'enc_edge_b': jnp.zeros((H,), jnp.float32), 'ln_g': jnp.ones((L, H), jnp.float32), 'ln_b': jnp.zeros((L, H), jnp.float32), 'mlp1_w': jax.random.normal(ks[5], (L, H, 2 * H), jnp.float32) * s, 'mlp1_b': jnp.zeros((L, 2 * H), jnp.float32), 'mlp_ln_g': jnp.ones((L, 2 * H), jnp.float32), 'mlp_ln_b': jnp.zeros((L, 2 * H), jnp.float32), 'mlp2_w': jax.random.normal(ks[6], (L, 2 * H, H), jnp.float32) * s, 'mlp2_b': jnp.zeros((L, H), jnp.float32), 't': jnp.ones((L,), jnp.float32)}
    _L0_gnn_all = _L0_gnn_setup()
    _L0_gnn_in = {k: v for k, v in _L0_gnn_all.items() if k in ('enc_node_w', 'enc_node_b', 'enc_edge_w', 'enc_edge_b', 'ln_g', 'ln_b', 'mlp1_w', 'mlp1_b', 'mlp_ln_g', 'mlp_ln_b', 'mlp2_w', 'mlp2_b', 't')}
    del _L0_gnn_all
    return {'x': x, 'src': src, 'dst': dst, 'edge_attr_64': edge_attr_64, 'L0_gnn_enc_node_w': _L0_gnn_in['enc_node_w'], 'L0_gnn_enc_node_b': _L0_gnn_in['enc_node_b'], 'L0_gnn_enc_edge_w': _L0_gnn_in['enc_edge_w'], 'L0_gnn_enc_edge_b': _L0_gnn_in['enc_edge_b'], 'L0_gnn_ln_g': _L0_gnn_in['ln_g'], 'L0_gnn_ln_b': _L0_gnn_in['ln_b'], 'L0_gnn_mlp1_w': _L0_gnn_in['mlp1_w'], 'L0_gnn_mlp1_b': _L0_gnn_in['mlp1_b'], 'L0_gnn_mlp_ln_g': _L0_gnn_in['mlp_ln_g'], 'L0_gnn_mlp_ln_b': _L0_gnn_in['mlp_ln_b'], 'L0_gnn_mlp2_w': _L0_gnn_in['mlp2_w'], 'L0_gnn_mlp2_b': _L0_gnn_in['mlp2_b'], 'L0_gnn_t': _L0_gnn_in['t']}

def reference(x, src, dst, edge_attr_64, L0_gnn_enc_node_w, L0_gnn_enc_node_b, L0_gnn_enc_edge_w, L0_gnn_enc_edge_b, L0_gnn_ln_g, L0_gnn_ln_b, L0_gnn_mlp1_w, L0_gnn_mlp1_b, L0_gnn_mlp_ln_g, L0_gnn_mlp_ln_b, L0_gnn_mlp2_w, L0_gnn_mlp2_b, L0_gnn_t):
    import jax
    import jax.numpy as jnp

    def _L0_gnn_ref(x, edge_index, edge_attr, enc_node_w, enc_node_b, enc_edge_w, enc_edge_b, ln_g, ln_b, mlp1_w, mlp1_b, mlp_ln_g, mlp_ln_b, mlp2_w, mlp2_b, t):
        import jax, jax.numpy as jnp
        import numpy as np
        N = 3125
        E = 50000
        C = 64
        H = 64
        L = 4
        EPS_MSG = 1e-07
        LN_EPS = 1e-05

        def _layernorm(x, g, b):
            mu = jnp.mean(x, axis=-1, keepdims=True)
            var = jnp.mean(jnp.square(x - mu), axis=-1, keepdims=True)
            return (x - mu) * jax.lax.rsqrt(var + LN_EPS) * g + b

        def _genconv(h, edge_attr, src, dst, w1, b1, g1, bb1, w2, b2, t):
            msg = jax.nn.relu(h[src] + edge_attr) + EPS_MSG
            m = msg * t
            seg_max = jax.lax.stop_gradient(jax.ops.segment_max(m, dst, num_segments=N))
            ex = jnp.exp(m - seg_max[dst])
            denom = jax.ops.segment_sum(ex, dst, num_segments=N)
            alpha = ex / (denom[dst] + 1e-16)
            agg = jax.ops.segment_sum(msg * alpha, dst, num_segments=N)
            out = h + agg
            z = jax.nn.relu(_layernorm(out @ w1 + b1, g1, bb1))
            return z @ w2 + b2
        src, dst = (edge_index[0], edge_index[1])
        h = x @ enc_node_w + enc_node_b
        e = edge_attr @ enc_edge_w + enc_edge_b
        h = _genconv(h, e, src, dst, mlp1_w[0], mlp1_b[0], mlp_ln_g[0], mlp_ln_b[0], mlp2_w[0], mlp2_b[0], t[0])
        for i in range(1, L):
            z = jax.nn.relu(_layernorm(h, ln_g[i], ln_b[i]))
            h = h + _genconv(z, e, src, dst, mlp1_w[i], mlp1_b[i], mlp_ln_g[i], mlp_ln_b[i], mlp2_w[i], mlp2_b[i], t[i])
        return jax.nn.relu(_layernorm(h, ln_g[0], ln_b[0]))
    edge_index = jnp.stack([src, dst])
    x = _layernorm(x + _L0_gnn_ref(x, edge_index, edge_attr_64, L0_gnn_enc_node_w, L0_gnn_enc_node_b, L0_gnn_enc_edge_w, L0_gnn_enc_edge_b, L0_gnn_ln_g, L0_gnn_ln_b, L0_gnn_mlp1_w, L0_gnn_mlp1_b, L0_gnn_mlp_ln_g, L0_gnn_mlp_ln_b, L0_gnn_mlp2_w, L0_gnn_mlp2_b, L0_gnn_t), axis=-1)
    return x

_drawn_inputs = setup_inputs


def setup_inputs(seed=0):
    import zlib

    import numpy as np

    out = dict(_drawn_inputs(seed))
    spreads = {'L0_gnn_enc_node_b': (0.0, 0.1),
     'L0_gnn_enc_edge_b': (0.0, 0.1),
     'L0_gnn_ln_g': (1.0, 0.2),
     'L0_gnn_ln_b': (0.0, 0.1),
     'L0_gnn_mlp1_b': (0.0, 0.1),
     'L0_gnn_mlp_ln_g': (1.0, 0.2),
     'L0_gnn_mlp_ln_b': (0.0, 0.1),
     'L0_gnn_mlp2_b': (0.0, 0.1),
     'L0_gnn_t': (1.0, 0.6)}
    factors = {}
    for name, (base, spread) in spreads.items():
        noise = np.random.default_rng([zlib.crc32(name.encode()), seed]).standard_normal(out[name].shape)
        drawn = base * np.exp(spread * noise) if base else spread * noise
        out[name] = jnp.asarray(drawn.astype(out[name].dtype))
    for name, factor in factors.items():
        out[name] = (out[name] * factor).astype(out[name].dtype)
    return out
```

```python
import concourse.bass as bass
from concourse import mybir
from contextlib import ExitStack

P = 128
F = 64
HID = 128
LAYERS = 4
NODES = 3125
EDGES = 103125
NT = -(-NODES // P)
NP_ROWS = NT * P
TG = 5
NG = NT // TG
HALVES = 2
CH = 512
KT = CH // P
SLOTS = 2
COLS = -(-(-(-EDGES // HALVES)) // (CH * SLOTS)) * CH * SLOTS
NCH = COLS // CH
NPAIR = NCH // SLOTS
EA = -(-EDGES // HALVES)
EB = EDGES - EA
PAD_TILES = (COLS - EA) // P
ROWS = P // HALVES
RC = COLS // ROWS
EPS_MSG = 1e-7
LN_EPS = 1e-5
BIG = 1.5e38
FAR = 1 << 20

assert NT == TG * NG and ROWS * RC == COLS and PAD_TILES < KT * SLOTS


def gnn_kernel(nc, x_nodes, x_t, dst_stream, src_tiles, attr_t, enc_node_w, enc_node_b, enc_edge_w, enc_edge_b,
               ln_g, ln_b, mlp1_w, mlp1_b, mlp_ln_g, mlp_ln_b, mlp2_w, mlp2_b, t_in,
               z_table, rows_table, keep_dram, keys_dram, out):
    f32, i32, u8 = mybir.dt.float32, mybir.dt.int32, mybir.dt.uint8
    ALU, ACT, AX = mybir.AluOpType, mybir.ActivationFunctionType, mybir.AxisListType

    dst_now = [dst_stream[h, 1:1 + COLS].rearrange("(r c) -> r c", c=RC) for h in range(HALVES)]
    dst_before = [dst_stream[h, 0:COLS].rearrange("(r c) -> r c", c=RC) for h in range(HALVES)]
    rows_by_chunk = rows_table.rearrange("(h c k p) e -> c h p k e", h=HALVES, c=NCH, k=KT)
    boundary_row = COLS - 1

    with ExitStack() as ctx:
        def sb(name, shape, dt=f32):
            return ctx.enter_context(nc.sbuf_tensor(name, shape, dt))

        def slots(name, shape, dt=f32):
            return [sb(f"{name}{s}", shape, dt) for s in range(SLOTS)]

        def sem(name):
            return ctx.enter_context(nc.semaphore(name))

        def sems(name):
            return [sem(f"{name}{s}") for s in range(SLOTS)]

        ident = sb("ident", [P, P])
        ones = sb("ones", [P, P])
        eps_col = sb("eps_col", [P, 1])
        enc_edge2 = sb("enc_edge2", [P, P])
        edge_bias = sb("edge_bias", [P, 1])
        enc_node = sb("enc_node", [F + 1, F])
        xT = sb("xT", [F + 1, NP_ROWS])
        w1 = sb("w1", [F + 1, HID])
        w2 = sb("w2", [HID, F])
        b2 = sb("b2", [1, F])
        g1c = sb("g1c", [HID, 1])
        b1c = sb("b1c", [HID, 1])
        lng = sb("lng", [P, F])
        lnb = sb("lnb", [P, F])
        tcol = sb("tcol", [P, 1])
        keep8 = sb("keep8", [P, COLS + 2], u8)
        idx = slots("idx", [P, KT * HALVES], i32)
        attr = slots("attr", [P, CH])
        gath = slots("gath", [P, KT * HALVES * F])
        msg = slots("msg", [P, CH])
        tm = slots("tm", [P, CH + 1])
        pen = slots("pen", [P, CH + 2])
        rmax = slots("rmax", [P, CH + 1])
        shift = slots("shift", [P, CH + 1])
        ex = slots("ex", [P, CH + 1])
        wmsg = sb("wmsg", [P, CH])
        carry = sb("carry", [P, 2])
        state = slots("state", [P, 2, CH])
        rows = slots("rows", [P, KT, HALVES, 2, F])
        ends = sb("ends", [1, 3 * P])
        ends_max = sb("ends_max", [1, F])
        ends_shift = sb("ends_shift", [1, P])
        ends_exp = sb("ends_exp", [1, P])
        ends_w = sb("ends_w", [1, 2, P])
        ends_row = sb("ends_row", [1, 2, F])
        x_sb = sb("x_sb", [P, NT, F])
        z_sb = sb("z_sb", [P, NT, F])
        h_sb = sb("h_sb", [P, NT, F])
        agg = sb("agg", [P, TG, 2 * F])
        na = sb("na", [P, TG, F])
        nb = sb("nb", [P, TG, F])
        node_in = sb("node_in", [P, TG, F + 1])
        inT = sb("inT", [F + 1, TG * P])
        stats = sb("stats", [P, TG, 6])
        mv = sb("mv", [P, TG, 2])
        sd = sb("sd", [P, TG])
        rstd = sb("rstd", [P, TG])
        idle = sb("idle", [P, 1])
        hid = sb("hid", [P, TG, HID])
        hidT = sb("hidT", [HID, TG * P])
        dnow = sb("dnow", [P, RC], i32)
        dbef = sb("dbef", [P, RC], i32)
        keepc = sb("keepc", [P, RC], u8)
        keys = sb("keys", [P, RC])
        sign = sb("sign", [P, 1])
        node_i = sb("node_i", [P, NT], i32)
        node_f = sb("node_f", [P, NT])
        last_i = sb("last_i", [P, 2], i32)
        last_f = sb("last_f", [P, 2])
        pen_same = sb("pen_same", [P, 1])
        in_a = sb("in_a", [P, NT])
        query = sb("query", [P, NT])
        diag = sb("diag", [P, P])
        below = sb("below", [P, NT, P])
        nbelow = sb("nbelow", [P, NT, HALVES])
        row_f = sb("row_f", [P, NT])
        row_i = sb("row_i", [P, NT], i32)
        row_g = sb("row_g", [P, TG], i32)
        key_rows = [sb(f"key_rows{i}", [P, RC]) for i in range(TG)]
        junk = sb("junk", [P, RC])
        cnt_le = sb("cnt_le", [P, NT])
        cnt_eq = sb("cnt_eq", [P, NT])
        has = sb("has", [P, NT])
        pos_f = sb("pos_f", [P, NT])
        pos_i = sb("pos_i", [P, NT], i32)
        pos_g = sb("pos_g", [P, TG], i32)

        px = [ctx.enter_context(nc.psum_tensor(f"px{s}", [P, CH], f32)) for s in range(SLOTS)]
        pt = [ctx.enter_context(nc.psum_tensor(f"pt{s}", [P, 2 * CH], f32)) for s in range(SLOTS)]

        settled = sem("settled")
        dst_landed, consts_landed, consts_set = sem("dst_landed"), sem("consts_landed"), sem("consts_set")
        pool_set, ident_set = sem("pool_set"), sem("ident_set")
        keep_ready, keep_stored, keep_landed = sem("keep_ready"), sem("keep_stored"), sem("keep_landed")
        keys_stored, prep = sem("keys_stored"), sem("prep")
        diag_ready, bounds_ready, h0_ready = sem("diag_ready"), sem("bounds_ready"), sem("h0_ready")
        rows_found, row_picked, keys_gathered = sem("rows_found"), sem("row_picked"), sem("keys_gathered")
        keys_counted, counted_le, pos_ready = sem("keys_counted"), sem("counted_le"), sem("pos_ready")
        z_ready, z_stored, params_landed = sem("z_ready"), sem("z_stored"), sem("params_landed")
        attr_landed, idx_landed, gathered = sems("attr_landed"), sems("idx_landed"), sems("gathered")
        x_ready, msg_ready, tm_ready, pen_ready = sems("x_ready"), sems("msg_ready"), sems("tm_ready"), sems("pen_ready")
        carried, run_max, seg_max, shifted = sems("carried"), sems("run_max"), sems("seg_max"), sems("shifted")
        exp_ready, carry_ready, weighted = sems("exp_ready"), sems("carry_ready"), sems("weighted")
        den_ready, num_ready = sems("den_ready"), sems("num_ready")
        state_t, rows_ready, stored = sems("state_t"), sems("rows_ready"), sems("stored")
        ends_t, ends_shifted, ends_exped, ends_step = sem("ends_t"), sem("ends_shifted"), sem("ends_exped"), sem("ends_step")
        ends_ready, ends_stored = sem("ends_ready"), sem("ends_stored")
        pos_picked, agg_gathered, agg_read, node_step = sem("pos_picked"), sem("agg_gathered"), sem("agg_read"), sem("node_step")
        in_ready, in_t, in_copied, a1_ready = sem("in_ready"), sem("in_t"), sem("in_copied"), sem("a1_ready")
        var_ready, sd_ready, hid_ready, hid_t, hid_copied = sem("var_ready"), sem("sd_ready"), sem("hid_ready"), sem("hid_t"), sem("hid_copied")
        conv_ready, var2_ready, sd2_ready = sem("conv_ready"), sem("var2_ready"), sem("sd2_ready")
        fvar_ready, fsd_ready, fin_step, out_stored = sem("fvar_ready"), sem("fsd_ready"), sem("fin_step"), sem("out_stored")

        block = ctx.enter_context(nc.Block())

        N_CONST = 10
        N_PARAM = 9

        @block.sync
        def _(sp):
            for h in range(HALVES):
                sp.dma_start(dnow[h * ROWS:(h + 1) * ROWS, :], dst_now[h]).then_inc(dst_landed, 16)
                sp.dma_start(dbef[h * ROWS:(h + 1) * ROWS, :], dst_before[h]).then_inc(dst_landed, 16)
                sp.dma_start(last_i[:, h:h + 1], dst_stream[h:h + 1, COLS:COLS + 1].broadcast_to([P, 1])).then_inc(dst_landed, 16)
            sp.wait_ge(consts_set, 3)
            sp.dma_start(xT[0:F, :], x_t).then_inc(consts_landed, 16)
            sp.dma_start(enc_node[0:F, :], enc_node_w).then_inc(consts_landed, 16)
            sp.dma_start(enc_node[F:F + 1, :], enc_node_b).then_inc(consts_landed, 16)
            for h in range(HALVES):
                sp.dma_start(enc_edge2[h * F:(h + 1) * F, h * F:(h + 1) * F], enc_edge_w).then_inc(consts_landed, 16)
                sp.dma_start(edge_bias[h * F:(h + 1) * F, :], enc_edge_b).then_inc(consts_landed, 16)
            sp.dma_start(x_sb[:, :, :], x_nodes).then_inc(consts_landed, 16)
            sp.wait_ge(z_ready, 2)
            sp.dma_start(z_table.rearrange("(t p) f -> p t f", p=P), z_sb[:, :, :]).then_inc(z_stored, 16)
            sp.wait_ge(keep_ready, 1)
            sp.dma_start(keep_dram, keepc[:, :]).then_inc(keep_stored, 16)
            sp.wait_ge(keep_ready, 2)
            sp.dma_start(keys_dram, keys[:, :]).then_inc(keys_stored, 16)
            sp.wait_ge(keep_stored, 16)
            for h in range(HALVES):
                sp.dma_start(keep8[h * F:(h + 1) * F, 1:1 + COLS],
                             keep_dram[h * ROWS:(h + 1) * ROWS, :].rearrange("(o r) c -> o (r c)", o=1).broadcast_to([F, COLS]))\
                    .then_inc(keep_landed, 16)

            def load(s, layer, pair, first=False):
                if not first:
                    sp.wait_ge(x_ready[s], layer * NPAIR + pair)
                c = pair * SLOTS + s
                sp.dma_start(idx[s][:, :], src_tiles[bass.ds(c * P, P), :]).then_inc(idx_landed[s], 16)
                sp.dma_start(attr[s][:, :], attr_t[bass.ds(c * P, P), :]).then_inc(attr_landed[s], 16)

            def store(s, layer, pair):
                sp.wait_ge(rows_ready[s], 2 * (layer * NPAIR + pair + 1))
                c = pair * SLOTS + s
                for h in range(HALVES):
                    dst = rows_by_chunk[bass.ds(c, 1), h].rearrange("o p k e -> (o p) k e")
                    sp.dma_start(dst, rows[s][:, :, h].rearrange("p k q f -> p k (q f)")).then_inc(stored[s], 16)

            with sp.Fori(0, LAYERS) as layer:
                sp.wait_ge(z_ready, 2 + layer * NG)
                sp.dma_start(w1[0:F, :], mlp1_w[bass.ds(layer * F, F), :]).then_inc(params_landed, 16)
                sp.dma_start(w1[F:F + 1, :], mlp1_b[bass.ds(layer, 1), :]).then_inc(params_landed, 16)
                sp.dma_start(w2[:, :], mlp2_w[bass.ds(layer * HID, HID), :]).then_inc(params_landed, 16)
                sp.dma_start(b2[:, :], mlp2_b[bass.ds(layer, 1), :]).then_inc(params_landed, 16)
                sp.dma_start(g1c[:, :], mlp_ln_g[bass.ds(layer * HID, HID), :]).then_inc(params_landed, 16)
                sp.dma_start(b1c[:, :], mlp_ln_b[bass.ds(layer * HID, HID), :]).then_inc(params_landed, 16)
                sp.dma_start(lng[:, :], ln_g[bass.ds(layer, 1), :].broadcast_to([P, F])).then_inc(params_landed, 16)
                sp.dma_start(lnb[:, :], ln_b[bass.ds(layer, 1), :].broadcast_to([P, F])).then_inc(params_landed, 16)
                sp.dma_start(tcol[:, :], t_in[bass.ds(layer, 1), :].broadcast_to([P, 1])).then_inc(params_landed, 16)
                for s in range(SLOTS):
                    load(s, layer, 0, first=True)
                load(0, layer, 1)
                load(1, layer, 1)
                store(0, layer, 0)
                with sp.Fori(1, NPAIR - 1) as pair:
                    load(0, layer, pair + 1)
                    store(1, layer, pair - 1)
                    load(1, layer, pair + 1)
                    store(0, layer, pair)
                store(1, layer, NPAIR - 2)
                store(0, layer, NPAIR - 1)
                store(1, layer, NPAIR - 1)
                for s in range(SLOTS):
                    sp.wait_ge(stored[s], 16 * HALVES * NPAIR * (layer + 1))
                sp.wait_ge(ends_ready, layer + 1)
                sp.dma_start(rows_table[boundary_row:boundary_row + 1, :],
                             ends_row[:, :, :].rearrange("o q f -> o (q f)")).then_inc(ends_stored, 16)
                with sp.Fori(0, NG) as g:
                    sp.wait_ge(z_ready, 2 + layer * NG + g + 1)
                    sp.dma_start(z_table[bass.ds(g * (TG * P), TG * P), :].rearrange("(t p) f -> p t f", p=P),
                                 z_sb[:, bass.ds(g * TG, TG), :]).then_inc(z_stored, 16)
            full = NODES // P
            sp.wait_ge(fin_step, NG)
            sp.dma_start(out[0:full * P, :].rearrange("(t p) f -> p t f", p=P), h_sb[:, 0:full, :]).then_inc(out_stored, 16)
            sp.dma_start(out[full * P:NODES, :], h_sb[0:NODES - full * P, full, :]).then_inc(out_stored, 16)
            sp.wait_ge(out_stored, 32)
            sp.wait_ge(z_stored, 16 * (1 + LAYERS * NG))

        @block.gpsimd
        def _(pool):
            nc.gpsimd.memset(ident[:, :], 0.0).then_inc(ident_set, 1)
            pool.wait_ge(ident_set, 1)
            nc.gpsimd.affine_select(out=ident[:, :], in_=ident[:, :], compare_op=ALU.not_equal, fill=1.0, base=0,
                                    pattern=[[-1, P]], channel_multiplier=1).then_inc(ident_set, 1)
            nc.gpsimd.iota(node_i[:, :], pattern=[[P, NT]], base=0, channel_multiplier=1).then_inc(pool_set, 1)
            for s in range(SLOTS):
                nc.gpsimd.memset(gath[s][:, :], 0.0).then_inc(pool_set, 1)

            def settle():
                pool.sem_inc(settled, 1)

            pool.wait_ge(ident_set, 2)
            pool.wait_ge(rows_found, 1)
            pool.wait_ge(keys_stored, 16)
            with pool.Fori(0, NG) as g:
                nc.gpsimd.tensor_copy(row_g[:, :], row_i[:, bass.ds(g * TG, TG)]).then_inc(row_picked, 1)
                pool.wait_ge(row_picked, g + 1)
                settle()
                for i in range(TG):
                    pool.indirect_dma_start(out=key_rows[i][:, :], out_offset=None, in_=keys_dram,
                                            in_offset=bass.IndirectOffsetOnAxis(ap=row_g[:, i:i + 1], axis=0))\
                        .then_inc(keys_gathered, 16)
                pool.wait_ge(keys_counted, (g + 1) * TG)

            def gather(s, first=0):
                for n in range(first * HALVES, KT * HALVES):
                    pool.indirect_dma_start(out=gath[s][:, n * F:(n + 1) * F], out_offset=None, in_=z_table,
                                            in_offset=bass.IndirectOffsetOnAxis(ap=idx[s][:, n:n + 1], axis=0))\
                        .then_inc(gathered[s], 16)

            def gather_slot(s, layer, pair, skip=None):
                use = layer * NPAIR + pair
                pool.wait_ge(idx_landed[s], 16 * (use + 1))
                if skip is None:
                    pool.wait_ge(x_ready[s], use)
                settle()
                gather(s, skip or 0)

            with pool.Fori(0, LAYERS) as layer:
                pool.wait_ge(z_stored, 16 * (1 + layer * NG))
                gather_slot(1, layer, 0, PAD_TILES - KT)
                with pool.Fori(1, NPAIR) as pair:
                    for s in range(SLOTS):
                        gather_slot(s, layer, pair)
                for s in range(SLOTS):
                    pool.wait_ge(stored[s], 16 * HALVES * NPAIR * (layer + 1))
                pool.wait_ge(ends_stored, 16 * (layer + 1))
                pool.wait_ge(pos_ready, 1)
                settle()
                with pool.Fori(0, NG) as g:
                    nc.gpsimd.tensor_copy(pos_g[:, :], pos_i[:, bass.ds(g * TG, TG)]).then_inc(pos_picked, 1)
                    pool.wait_ge(pos_picked, layer * NG + g + 1)
                    settle()
                    for i in range(TG):
                        pool.indirect_dma_start(out=agg[:, i, :], out_offset=None, in_=rows_table,
                                                in_offset=bass.IndirectOffsetOnAxis(ap=pos_g[:, i:i + 1], axis=0))\
                            .then_inc(agg_gathered, 16)
                    pool.wait_ge(agg_read, layer * NG + g + 1)

        @block.tensor
        def _(pe):
            pe.wait_ge(diag_ready, 1)
            nc.tensor.matmul(px[0][:, 0:P], ones[:, :], diag[:, :], start=True, stop=True).then_inc(bounds_ready, 1)
            pe.wait_ge(consts_landed, 16 * 8)
            split = 2 * CH // F
            for t in range(NT):
                dst = pt[t // split][:, (t % split) * F:(t % split + 1) * F]
                last = nc.tensor.matmul(dst, xT[:, t * P:(t + 1) * P], enc_node[:, :], start=True, stop=True)
                if t in (split - 1, NT - 1):
                    last.then_inc(h0_ready, 1)

            def edge_sum(s, layer, pair, filled, first=False):
                use = layer * NPAIR + pair
                pe.wait_ge(attr_landed[s], 16 * (use + 1))
                if not first:
                    pe.wait_ge(msg_ready[s], use)
                nc.tensor.matmul(px[s][:, :], enc_edge2[:, :], attr[s][:, :], start=True, stop=False)
                if filled is not None:
                    pe.wait_ge(gathered[s], filled)
                for k in range(KT):
                    last = nc.tensor.matmul(px[s][:, k * P:(k + 1) * P], gath[s][:, k * P:(k + 1) * P], ident[:, :],
                                            start=False, stop=(k == KT - 1))
                last.then_inc(x_ready[s], 1)

            per_layer = [16 * HALVES * KT * (NPAIR - 1), 16 * HALVES * (KT * NPAIR - (PAD_TILES - KT))]

            def filled(s, layer, pair):
                if s == 0:
                    return layer * per_layer[0] + pair * (16 * HALVES * KT)
                return layer * per_layer[1] + (pair + 1) * (16 * HALVES * KT) - 16 * HALVES * (PAD_TILES - KT)

            def turn_states(s, layer, pair, first=False):
                use = layer * NPAIR + pair
                pe.wait_ge(den_ready[s], use + 1)
                pe.wait_ge(num_ready[s], use + 1)
                if not first:
                    pe.wait_ge(rows_ready[s], 2 * use)
                for q in range(2):
                    for k in range(KT):
                        last = nc.tensor.transpose(pt[s][:, q * CH + k * P:q * CH + (k + 1) * P],
                                                   state[s][:, q, k * P:(k + 1) * P], ident[:, :])
                last.then_inc(state_t[s], 1)

            with pe.Fori(0, LAYERS) as layer:
                pe.wait_ge(pool_set, 1 + SLOTS)
                pe.wait_ge(params_landed, 16 * N_PARAM * (layer + 1))
                edge_sum(0, layer, 0, None, first=True)
                edge_sum(1, layer, 0, filled(1, layer, 0), first=True)
                turn_states(0, layer, 0, first=True)
                edge_sum(0, layer, 1, filled(0, layer, 1))
                turn_states(1, layer, 0, first=True)
                edge_sum(1, layer, 1, filled(1, layer, 1))
                turn_states(0, layer, 1)
                with pe.Fori(2, NPAIR) as pair:
                    edge_sum(0, layer, pair, filled(0, layer, pair))
                    turn_states(1, layer, pair - 1)
                    edge_sum(1, layer, pair, filled(1, layer, pair))
                    turn_states(0, layer, pair)
                turn_states(1, layer, NPAIR - 1)
                last_col = [rmax[1][:, CH:CH + 1], state[1][:, 0, CH - 1:CH], state[1][:, 1, CH - 1:CH]]
                for n, col in enumerate(last_col):
                    last = nc.tensor.matmul(px[1][0:1, n * P:(n + 1) * P], col, ident[:, :], start=True, stop=True)
                last.then_inc(ends_t, 1)
                with pe.Fori(0, NG) as g:
                    q = layer * NG + g
                    pe.wait_ge(in_ready, q + 1)
                    for i in range(TG):
                        last = nc.tensor.transpose(pt[0][0:F + 1, i * P:(i + 1) * P], node_in[:, i, :], ident[:, :])
                    last.then_inc(in_t, 1)
                    pe.wait_ge(in_copied, q + 1)
                    for i in range(TG):
                        last = nc.tensor.matmul(pt[1][:, i * HID:(i + 1) * HID], inT[:, i * P:(i + 1) * P], w1[:, :],
                                                start=True, stop=True)
                    last.then_inc(a1_ready, 1)
                    pe.wait_ge(hid_ready, q + 1)
                    for i in range(TG):
                        last = nc.tensor.transpose(pt[0][:, i * P:(i + 1) * P], hid[:, i, :], ident[:, :])
                    last.then_inc(hid_t, 1)
                    pe.wait_ge(hid_copied, q + 1)
                    for i in range(TG):
                        dst = px[0][:, i * F:(i + 1) * F]
                        nc.tensor.matmul(dst, hidT[:, i * P:(i + 1) * P], w2[:, :], start=True, stop=False)
                        last = nc.tensor.matmul(dst, ones[0:1, :], b2[:, :], start=False, stop=True)
                    last.then_inc(conv_ready, 1)

        @block.scalar
        def _(act):
            def messages(s, layer, pair, first=False):
                use = layer * NPAIR + pair
                c = pair * SLOTS + s
                if not first:
                    act.wait_ge(seg_max[s], use)
                nc.scalar.activation(pen[s][:, :], keep8[:, bass.ds(c * CH, CH + 2)], ACT.Copy,
                                     scale=BIG, bias=-BIG).then_inc(pen_ready[s], 1)
                act.wait_ge(x_ready[s], use + 1)
                if not first:
                    act.wait_ge(weighted[s], use)
                nc.scalar.activation(msg[s][:, :], px[s][:, :], ACT.Relu, bias=edge_bias[:, :]).then_inc(msg_ready[s], 1)
                act.wait_ge(msg_ready[s], use + 1)
                if not first:
                    act.wait_ge(shifted[s], use)
                nc.scalar.activation(tm[s][:, 1:1 + CH], msg[s][:, :], ACT.Copy, scale=tcol[:, :]).then_inc(tm_ready[s], 1)
                act.wait_ge(shifted[s], use + 1)
                if not first:
                    act.wait_ge(den_ready[s], use)
                nc.scalar.activation(ex[s][:, :], shift[s][:, :], ACT.Exp).then_inc(exp_ready[s], 1)

            def copy_rows(s, layer, pair, first=False):
                use = layer * NPAIR + pair
                act.wait_ge(state_t[s], use + 1)
                if not first:
                    act.wait_ge(stored[s], 16 * HALVES * use)
                for q in range(2):
                    nc.scalar.activation(rows[s][:, :, :, q, :],
                                         pt[s][:, q * CH:(q + 1) * CH].rearrange("p (k h f) -> p k h f", k=KT, h=HALVES),
                                         ACT.Copy).then_inc(rows_ready[s], 1)

            act.wait_ge(consts_landed, 16 * 8)
            act.wait_ge(keep_landed, 32)
            act.wait_ge(consts_set, 6)
            with act.Fori(0, LAYERS) as layer:
                act.wait_ge(params_landed, 16 * N_PARAM * (layer + 1))
                messages(0, layer, 0, first=True)
                messages(1, layer, 0, first=True)
                copy_rows(0, layer, 0, first=True)
                messages(0, layer, 1)
                copy_rows(1, layer, 0, first=True)
                messages(1, layer, 1)
                copy_rows(0, layer, 1)
                with act.Fori(2, NPAIR) as pair:
                    messages(0, layer, pair)
                    copy_rows(1, layer, pair - 1)
                    messages(1, layer, pair)
                    copy_rows(0, layer, pair)
                copy_rows(1, layer, NPAIR - 1)
                act.wait_ge(ends_shifted, layer + 1)
                nc.scalar.activation(ends_exp[:, :], ends_shift[:, :], ACT.Exp).then_inc(ends_exped, 1)
                with act.Fori(0, NG) as g:
                    q = layer * NG + g
                    act.wait_ge(in_t, q + 1)
                    nc.scalar.activation(inT[:, :], pt[0][0:F + 1, 0:TG * P], ACT.Copy).then_inc(in_copied, 1)
                    act.wait_ge(var_ready, q + 1)
                    nc.scalar.activation(sd[:, :], mv[:, :, 1], ACT.Sqrt, bias=eps_col[:, :]).then_inc(sd_ready, 1)
                    act.wait_ge(hid_t, q + 1)
                    nc.scalar.activation(hidT[:, :], pt[0][:, 0:TG * P], ACT.Relu, bias=b1c[:, :], scale=g1c[:, :])\
                        .then_inc(hid_copied, 1)
                    act.wait_ge(var2_ready, q + 1)
                    nc.scalar.activation(sd[:, :], mv[:, :, 1], ACT.Sqrt, bias=eps_col[:, :]).then_inc(sd2_ready, 1)
            with act.Fori(0, NG) as g:
                act.wait_ge(fvar_ready, g + 1)
                nc.scalar.activation(sd[:, :], mv[:, :, 1], ACT.Sqrt, bias=eps_col[:, :]).then_inc(fsd_ready, 1)

        @block.vector
        def _(dve):
            v = nc.vector

            class Steps:
                def __init__(self, s, base=0):
                    self.s, self.base, self.n = s, base, 0

                def mark(self, ins):
                    self.n += 1
                    ins.then_inc(self.s, 1)

                def wait(self):
                    dve.wait_ge(self.s, self.base + self.n)

                def link(self, ins):
                    self.mark(ins)
                    self.wait()

            v.memset(enc_edge2[:, :], 0.0).then_inc(consts_set, 1)
            v.memset(xT[F:F + 1, :], 1.0).then_inc(consts_set, 1)
            v.memset(ones[:, :], 1.0).then_inc(consts_set, 1)
            v.memset(eps_col[:, :], LN_EPS).then_inc(consts_set, 1)
            v.memset(keep8[:, 0:1], 0).then_inc(consts_set, 1)
            v.memset(keep8[:, COLS + 1:COLS + 2], 0).then_inc(consts_set, 1)
            p = Steps(prep)
            p.mark(v.memset(rmax[1][:, CH:CH + 1], 0.0))
            p.mark(v.memset(state[1][:, :, CH - 1:CH], 0.0))
            p.mark(v.memset(node_in[:, :, F:F + 1], 1.0))
            p.mark(v.memset(h_sb[:, :, :], 0.0))
            p.mark(v.memset(sign[0:ROWS, :], 1.0))
            p.link(v.memset(sign[ROWS:P, :], -1.0))
            dve.wait_ge(dst_landed, 16 * 3 * HALVES)
            v.tensor_tensor(keepc[:, :], dnow[:, :], dbef[:, :], ALU.is_equal).then_inc(keep_ready, 1)
            v.tensor_scalar(keys[:, :], dnow[:, :], sign[:, :], None, ALU.mult).then_inc(keep_ready, 1)
            dve.wait_ge(ident_set, 2)
            dve.wait_ge(keep_ready, 2)
            v.tensor_scalar(diag[:, :], ident[:, :], keys[:, 0:1], None, ALU.mult).then_inc(diag_ready, 1)
            dve.wait_ge(pool_set, 1)
            p.mark(v.tensor_copy(node_f[:, :], node_i[:, :]))
            p.link(v.tensor_copy(last_f[:, :], last_i[:, :]))
            p.link(v.tensor_tensor(pen_same[:, :], last_f[:, 0:1], last_f[:, 1:2], ALU.is_equal))
            p.mark(v.tensor_scalar(pen_same[:, :], pen_same[:, :], BIG, -BIG, ALU.mult, ALU.add))
            p.link(v.tensor_scalar(in_a[:, :], node_f[:, :], last_f[:, 0:1], None, ALU.is_le))
            p.link(v.tensor_scalar(query[:, :], in_a[:, :], 2.0, -1.0, ALU.mult, ALU.add))
            p.link(v.tensor_tensor(query[:, :], query[:, :], node_f[:, :], ALU.mult))
            dve.wait_ge(bounds_ready, 1)
            p.link(v.tensor_tensor(below[:, :, :], px[0][:, 0:P].unsqueeze(1).broadcast_to([P, NT, P]),
                                   query[:, :].unsqueeze(2).broadcast_to([P, NT, P]), ALU.is_le))
            p.link(v.tensor_reduce(out=nbelow[:, :, :], in_=below[:, :, :].rearrange("p t (h r) -> p t h r", h=HALVES),
                                   op=ALU.add, axis=AX.X))
            p.link(v.tensor_tensor(row_f[:, :], nbelow[:, :, 0], nbelow[:, :, 1], ALU.subtract))
            p.link(v.tensor_scalar(row_f[:, :], row_f[:, :], float(-ROWS), None, ALU.add))
            p.link(v.tensor_tensor(row_f[:, :], row_f[:, :], in_a[:, :], ALU.mult))
            p.link(v.tensor_tensor(row_f[:, :], row_f[:, :], nbelow[:, :, 1], ALU.add))
            p.link(v.tensor_scalar(row_f[:, :], row_f[:, :], float(ROWS - 1), None, ALU.add))
            v.tensor_copy(row_i[:, :], row_f[:, :]).then_inc(rows_found, 1)
            split = 2 * CH // F
            dve.wait_ge(h0_ready, 2)
            v.tensor_copy(z_sb[:, 0:split, :], pt[0][:, 0:split * F].rearrange("p (t f) -> p t f", f=F)).then_inc(z_ready, 1)
            v.tensor_copy(z_sb[:, split:NT, :], pt[1][:, 0:(NT - split) * F].rearrange("p (t f) -> p t f", f=F))\
                .then_inc(z_ready, 1)
            with dve.Fori(0, NG) as g:
                dve.wait_ge(keys_gathered, 16 * TG * (g + 1))
                for i in range(TG):
                    q = query[:, bass.ds(g * TG + i, 1)]
                    v.tensor_scalar(junk[:, :], key_rows[i][:, :], q, None, ALU.is_le, ALU.add,
                                    accum_out=cnt_le[:, bass.ds(g * TG + i, 1)]).then_inc(counted_le, 1)
                    dve.wait_ge(counted_le, g * TG + i + 1)
                    v.tensor_scalar(junk[:, :], key_rows[i][:, :], q, None, ALU.is_equal, ALU.add,
                                    accum_out=cnt_eq[:, bass.ds(g * TG + i, 1)]).then_inc(keys_counted, 1)
                    dve.wait_ge(keys_counted, g * TG + i + 1)
            dve.wait_ge(keys_counted, NT)
            dve.wait_ge(rows_found, 1)
            p.mark(v.tensor_scalar(has[:, :], cnt_eq[:, :], 1.0, None, ALU.min))
            p.link(v.tensor_scalar(pos_f[:, :], row_f[:, :], float(RC), -1.0, ALU.mult, ALU.add))
            p.link(v.tensor_tensor(pos_f[:, :], pos_f[:, :], cnt_le[:, :], ALU.add))
            v.tensor_copy(pos_i[:, :], pos_f[:, :]).then_inc(pos_ready, 1)

            def softmax_sums(s, layer, pair, first=False):
                o = 1 - s
                use = layer * NPAIR + pair
                other = use + s
                c = pair * SLOTS + s
                if not (first and s == 0):
                    dve.wait_ge(run_max[o], other)
                if not first:
                    dve.wait_ge(shifted[s], use)
                v.tensor_copy(tm[s][:, 0:1], rmax[o][:, CH:CH + 1]).then_inc(carried[s], 1)
                dve.wait_ge(carried[s], use + 1)
                dve.wait_ge(tm_ready[s], use + 1)
                dve.wait_ge(pen_ready[s], use + 1)
                v.tensor_tensor_scan(out=rmax[s][:, :], data0=pen[s][:, 0:CH + 1], data1=tm[s][:, :], initial=-BIG,
                                     op0=ALU.add, op1=ALU.max).then_inc(run_max[s], 1)
                dve.wait_ge(run_max[s], use + 1)
                if not first:
                    dve.wait_ge(exp_ready[s], use)
                v.tensor_tensor_scan(out=shift[s][:, ::-1], data0=pen[s][:, 1:CH + 2][:, ::-1], data1=rmax[s][:, ::-1],
                                     initial=-BIG, op0=ALU.add, op1=ALU.max).then_inc(seg_max[s], 1)
                dve.wait_ge(seg_max[s], use + 1)
                v.tensor_tensor(shift[s][:, :], tm[s][:, :], shift[s][:, :], ALU.subtract).then_inc(shifted[s], 1)
                dve.wait_ge(exp_ready[s], use + 1)
                if not (first and s == 0):
                    dve.wait_ge(num_ready[o], other)
                v.tensor_scalar(carry[:, :], state[o][:, :, CH - 1], ex[s][:, 0:1], None, ALU.mult).then_inc(carry_ready[s], 1)
                v.tensor_tensor(wmsg[:, :], ex[s][:, 1:CH + 1], msg[s][:, :], ALU.mult).then_inc(weighted[s], 1)
                keep = keep8[:, bass.ds(c * CH + 1, CH)]
                dve.wait_ge(carry_ready[s], use + 1)
                if not first:
                    dve.wait_ge(state_t[s], use)
                v.tensor_tensor_scan(out=state[s][:, 0, :], data0=keep, data1=ex[s][:, 1:CH + 1], initial=carry[:, 0:1],
                                     op0=ALU.mult, op1=ALU.add).then_inc(den_ready[s], 1)
                dve.wait_ge(weighted[s], use + 1)
                v.tensor_tensor_scan(out=state[s][:, 1, :], data0=keep, data1=wmsg[:, :], initial=carry[:, 1:2],
                                     op0=ALU.mult, op1=ALU.add).then_inc(num_ready[s], 1)

            def statistics(st, src, done):
                for i in range(TG):
                    st.mark(v.bn_stats(out=stats[:, i, :], in_=src(i)))
                st.wait()
                v.memset(idle[:, :], 0.0)
                for i in range(TG):
                    last = v.bn_aggr(out=mv[:, i, :], in_=stats[:, i, :])
                    if i < TG - 1:
                        st.mark(last)
                last.then_inc(done, 1)

            def normalise(st, src, dst, sd_done, count):
                dve.wait_ge(sd_done, count)
                st.link(v.reciprocal(rstd[:, :], sd[:, :]))
                for i in range(TG):
                    last = v.tensor_scalar(dst(i), src(i), mv[:, i, 0:1], rstd[:, i:i + 1], ALU.subtract, ALU.mult)
                    if i < TG - 1:
                        st.mark(last)
                return last

            NODE_STEPS, FINAL_STEPS = 37, 15
            with dve.Fori(0, LAYERS) as layer:
                dve.wait_ge(keep_landed, 32)
                for s in range(SLOTS):
                    softmax_sums(s, layer, 0, first=True)
                with dve.Fori(1, NPAIR) as pair:
                    for s in range(SLOTS):
                        softmax_sums(s, layer, pair)
                e = Steps(ends_step, layer * 7)
                dve.wait_ge(params_landed, 16 * N_PARAM * (layer + 1))
                dve.wait_ge(ends_t, layer + 1)
                e.link(v.tensor_copy(ends[:, :], px[1][0:1, 0:3 * P]))
                e.link(v.tensor_scalar(ends[:, F:P], ends[:, F:P], pen_same[0:1, :], None, ALU.add))
                e.link(v.tensor_tensor(ends_max[:, :], ends[:, 0:F], ends[:, F:P], ALU.max))
                e.mark(v.tensor_tensor(ends_shift[:, 0:F], ends[:, 0:F], ends_max[:, :], ALU.subtract))
                v.tensor_tensor(ends_shift[:, F:P], ends[:, F:P], ends_max[:, :], ALU.subtract).then_inc(ends_shifted, 1)
                dve.wait_ge(ends_exped, layer + 1)
                e.mark(v.tensor_tensor(ends_w[:, 0, :], ends[:, P:2 * P], ends_exp[:, :], ALU.mult))
                e.link(v.tensor_tensor(ends_w[:, 1, :], ends[:, 2 * P:3 * P], ends_exp[:, :], ALU.mult))
                v.tensor_tensor(ends_row[:, :, :], ends_w[:, :, 0:F], ends_w[:, :, F:P], ALU.add).then_inc(ends_ready, 1)
                e.mark(v.memset(ends_max[:, :], 0.0))
                assert e.n == 7

                with dve.Fori(0, NG) as g:
                    q = layer * NG + g
                    st = Steps(node_step, q * NODE_STEPS)
                    tiles = bass.ds(g * TG, TG)
                    dve.wait_ge(agg_gathered, 16 * TG * (q + 1))
                    den, num = agg[:, :, 0:F], agg[:, :, F:2 * F]
                    st.mark(v.scalar_tensor_tensor(out=na[:, :, :], in0=den, scalar=EPS_MSG, in1=num, op0=ALU.mult, op1=ALU.add))
                    v.tensor_scalar(nb[:, :, :], den, 1e-16, None, ALU.add).then_inc(agg_read, 1)
                    dve.wait_ge(agg_read, q + 1)
                    st.link(v.reciprocal(nb[:, :, :], nb[:, :, :]))
                    st.link(v.tensor_tensor(na[:, :, :], na[:, :, :], nb[:, :, :], ALU.mult))
                    st.link(v.tensor_tensor(na[:, :, :], na[:, :, :], has[:, tiles].unsqueeze(2).broadcast_to([P, TG, F]), ALU.mult))
                    v.tensor_tensor(node_in[:, :, 0:F], na[:, :, :], z_sb[:, tiles, :], ALU.add).then_inc(in_ready, 1)
                    dve.wait_ge(a1_ready, q + 1)
                    hidden = lambda i: pt[1][:, i * HID:(i + 1) * HID]
                    statistics(st, hidden, var_ready)
                    normalise(st, hidden, lambda i: hid[:, i, :], sd_ready, q + 1).then_inc(hid_ready, 1)
                    dve.wait_ge(conv_ready, q + 1)
                    st.link(v.tensor_tensor(nb[:, :, :], h_sb[:, tiles, :],
                                            px[0][:, 0:TG * F].rearrange("p (t f) -> p t f", f=F), ALU.add))
                    row = lambda i: nb[:, i, :]
                    statistics(st, row, var2_ready)
                    st.mark(v.tensor_copy(h_sb[:, tiles, :], nb[:, :, :]))
                    st.link(normalise(st, row, lambda i: na[:, i, :], sd2_ready, q + 1))
                    st.link(v.tensor_tensor(na[:, :, :], na[:, :, :], lng[:, :].unsqueeze(1).broadcast_to([P, TG, F]), ALU.mult))
                    st.link(v.tensor_tensor(na[:, :, :], na[:, :, :], lnb[:, :].unsqueeze(1).broadcast_to([P, TG, F]), ALU.add))
                    v.tensor_scalar(z_sb[:, tiles, :], na[:, :, :], 0.0, None, ALU.max).then_inc(z_ready, 1)
                    assert st.n == NODE_STEPS, st.n
                    dve.wait_ge(z_ready, 2 + q + 1)
            with dve.Fori(0, NG) as g:
                st = Steps(node_step, LAYERS * NG * NODE_STEPS + g * FINAL_STEPS)
                tiles = bass.ds(g * TG, TG)
                dve.wait_ge(z_ready, 2 + LAYERS * NG)
                dve.wait_ge(consts_landed, 16 * 8)
                st.link(v.tensor_tensor(na[:, :, :], x_sb[:, tiles, :], z_sb[:, tiles, :], ALU.add))
                statistics(st, lambda i: na[:, i, :], fvar_ready)
                last = normalise(st, lambda i: na[:, i, :],
                                 lambda i: h_sb[:, bass.ds(g * TG + i, 1), :].rearrange("p o f -> p (o f)"), fsd_ready, g + 1)
                last.then_inc(fin_step, 1)
                assert st.n == FINAL_STEPS, st.n
                dve.wait_ge(fin_step, g + 1)


def kernel(x, src, dst, edge_attr_64, L0_gnn_enc_node_w, L0_gnn_enc_node_b, L0_gnn_enc_edge_w, L0_gnn_enc_edge_b,
           L0_gnn_ln_g, L0_gnn_ln_b, L0_gnn_mlp1_w, L0_gnn_mlp1_b, L0_gnn_mlp_ln_g, L0_gnn_mlp_ln_b, L0_gnn_mlp2_w,
           L0_gnn_mlp2_b, L0_gnn_t):
    import numpy as np
    import concourse.bacc as bacc
    from concourse.bass_utils import run_bass_kernel_spmd

    def arr(a):
        return np.asarray(a)

    x, src, dst, attr = arr(x), arr(src), arr(dst), arr(edge_attr_64)
    x_pad = np.zeros((NP_ROWS, F), x.dtype)
    x_pad[:NODES] = x

    def streams(a, front):
        s = np.zeros((HALVES, front + COLS) + a.shape[1:], a.dtype)
        s[0, front + COLS - EA:] = a[:EA]
        s[1, front + COLS - EB:] = a[EA:][::-1]
        return s

    dst_s = streams(dst, 1)
    dst_s[0, :1 + COLS - EA] = -1
    dst_s[1, :1 + COLS - EB] = FAR
    dst_s[0, 0], dst_s[1, 0] = -2, 2 * FAR
    src_s = streams(src, 0).reshape(HALVES, NCH, KT, P).transpose(1, 3, 2, 0).reshape(NCH * P, KT * HALVES)
    attr_s = streams(attr, 0).reshape(HALVES, NCH, CH, F).transpose(1, 0, 3, 2).reshape(NCH * P, CH)
    nxt = list(range(1, LAYERS)) + [0]
    arrays = {
        "x_nodes": x_pad.reshape(NT, P, F).transpose(1, 0, 2),
        "x_t": x_pad.T,
        "dst_stream": dst_s,
        "src_tiles": src_s,
        "attr_t": attr_s,
        "enc_node_w": arr(L0_gnn_enc_node_w),
        "enc_node_b": arr(L0_gnn_enc_node_b).reshape(1, F),
        "enc_edge_w": arr(L0_gnn_enc_edge_w),
        "enc_edge_b": arr(L0_gnn_enc_edge_b).reshape(F, 1),
        "ln_g": arr(L0_gnn_ln_g)[nxt],
        "ln_b": arr(L0_gnn_ln_b)[nxt],
        "mlp1_w": arr(L0_gnn_mlp1_w).reshape(LAYERS * F, HID),
        "mlp1_b": arr(L0_gnn_mlp1_b),
        "mlp_ln_g": arr(L0_gnn_mlp_ln_g).reshape(LAYERS * HID, 1),
        "mlp_ln_b": arr(L0_gnn_mlp_ln_b).reshape(LAYERS * HID, 1),
        "mlp2_w": arr(L0_gnn_mlp2_w).reshape(LAYERS * HID, F),
        "mlp2_b": arr(L0_gnn_mlp2_b),
        "t_in": arr(L0_gnn_t).reshape(LAYERS, 1),
    }
    arrays = {k: np.ascontiguousarray(a) for k, a in arrays.items()}
    nc = bacc.Bacc("TRN2", target_bir_lowering=False, num_devices=1)
    args = [nc.dram_tensor(k, a.shape, mybir.dt.from_np(a.dtype), kind="ExternalInput").ap() for k, a in arrays.items()]
    f32 = mybir.dt.float32
    args.append(nc.dram_tensor("z_table", (NP_ROWS, F), f32).ap())
    args.append(nc.dram_tensor("rows_table", (HALVES * COLS, 2 * F), f32).ap())
    args.append(nc.dram_tensor("keep_dram", (P, RC), mybir.dt.uint8).ap())
    args.append(nc.dram_tensor("keys_dram", (P, RC), f32).ap())
    args.append(nc.dram_tensor("y_out", (NODES, F), f32, kind="ExternalOutput").ap())
    gnn_kernel(nc, *args)
    r = run_bass_kernel_spmd(nc, [arrays], core_ids=[0])
    return r.results[0]["y_out"]
```
